# Optimizing a Trainium2 kernel written in Bass

```python
import numpy as np
import jax
import jax.numpy as jnp

def _softmax(x, axis=-1):
    return jax.nn.softmax(x, axis=axis)

def _gelu(x):
    return jax.nn.gelu(x, approximate=True)

def _silu(x):
    return jax.nn.silu(x)

def _sigmoid(x):
    return jax.nn.sigmoid(x)

def _layernorm(x, axis=-1, eps=1e-05):
    m = jnp.mean(x, axis=axis, keepdims=True)
    v = jnp.var(x, axis=axis, keepdims=True)
    return (x - m) / jnp.sqrt(v + eps)

def _scatter_add(tgt, idx, src, axis=0):
    return tgt.at[idx].add(src)

def _segment_sum(src, seg, n):
    return jax.ops.segment_sum(src, seg, n)
kernel_name = 'mk_vit_tower_d1_tok_img512_r4_b47b0b'

def setup_inputs(seed: int=0):
    np.random.seed(seed)
    _w = jnp.asarray

    def _rec_inputs():
        import jax
        import jax.numpy as jnp
        _rk = jax.random.key(seed)
        x = -0.000147625 + 0.999875 * jax.random.normal(jax.random.fold_in(_rk, 1), (128, 3, 224, 224), jnp.float32)
        return x
    x = _rec_inputs()

    def _L0_tok_setup():
        import jax, jax.numpy as jnp
        import numpy as np
        N_PATCHES = 8
        PATCH = 28
        C = 3
        IN_D = C * PATCH * PATCH
        HID = 128
        SEQ = N_PATCHES * N_PATCHES + 1

        def _positional_embedding(seq_len, dim):
            i = np.arange(seq_len)[:, None].astype(np.float32)
            j = np.arange(dim)[None, :].astype(np.float32)
            ang = i / np.power(100000.0, j / dim)
            pe = np.where(j % 2 == 0, np.sin(ang), np.cos(ang))
            return jnp.asarray(pe, dtype=jnp.float32)
        key = jax.random.key(seed)
        k1, k2, k3, k4 = jax.random.split(key, 4)
        B = 64
        X = jax.random.normal(k1, (B, C, 224, 224), dtype=jnp.float32)
        bound = 1.0 / np.sqrt(IN_D)
        W = jax.random.uniform(k2, (HID, IN_D), minval=-bound, maxval=bound, dtype=jnp.float32)
        b = jax.random.uniform(k3, (HID,), minval=-bound, maxval=bound, dtype=jnp.float32)
        class_token = jax.random.uniform(k4, (1, HID), dtype=jnp.float32)
        pos_embed = _positional_embedding(SEQ, HID)
        return {'X': X, 'W': W, 'b': b, 'class_token': class_token, 'pos_embed': pos_embed}
    _L0_tok_all = _L0_tok_setup()
    _L0_tok_in = {k: v for k, v in _L0_tok_all.items() if k in ('W', 'b', 'class_token', 'pos_embed')}
    del _L0_tok_all

    def _L0_attn_setup():
        import jax, jax.numpy as jnp
        import numpy as np
        L, B = (512, 8)
        SIZE, NUM_HEADS, QK, V, MAXPOS = (128, 4, 128, 256, 512)
        LN_EPS = 1e-05

        def _multihead_damped_ema(x, p_raw, a_raw, beta, gamma, omega):
            length = x.shape[0]
            residual = x * omega
            xT = jnp.transpose(x, (1, 2, 0))
            p = jax.nn.sigmoid(p_raw)
            q = 1.0 - p * jax.nn.sigmoid(a_raw)
            vander = jnp.arange(length, dtype=x.dtype)[None, None, :] * jnp.log(q)
            kernel = p * beta * jnp.exp(vander)
            scaling = gamma.shape[1] ** (-0.5)
            k = jnp.einsum('dhl,dh->dl', kernel, gamma * scaling)
            n = 2 * length
            out = jnp.fft.irfft(jnp.fft.rfft(xT, n=n) * jnp.fft.rfft(k, n=n), n=n)[..., :length]
            return jax.nn.relu(jnp.transpose(out, (2, 0, 1)) + residual)

        def _simple_rel_pos_bias(w, length, max_positions):
            rel = jnp.arange(length)[None, :] - jnp.arange(length)[:, None]
            return w[max_positions - 1 + rel]
        key = jax.random.key(seed)
        ks = jax.random.split(key, 16)
        n = lambda k, sh, s=0.02: jax.random.normal(k, sh, dtype=jnp.float32) * s
        return {'x': jax.random.normal(ks[0], (L, B, SIZE), dtype=jnp.float32), 'proj_v_w': n(ks[1], (V, SIZE)), 'proj_v_b': jnp.zeros((V,), jnp.float32), 'proj_mx_w': n(ks[2], (QK + V + 2 * SIZE, SIZE)), 'proj_mx_b': jnp.zeros((QK + V + 2 * SIZE,), jnp.float32), 'proj_h_w': n(ks[3], (SIZE, V)), 'proj_h_b': jnp.zeros((SIZE,), jnp.float32), 'qk_weight': n(ks[4], (2, QK)), 'qk_bias': jnp.zeros((2, QK), jnp.float32), 'damping_factor': n(ks[5], (SIZE, NUM_HEADS, 1), 0.2), 'decay_factor': n(ks[6], (SIZE, NUM_HEADS, 1), 0.2), 'ema_expansion': n(ks[7], (SIZE, NUM_HEADS, 1), 1.0), 'ema_kernel_proj': n(ks[8], (SIZE, NUM_HEADS), 1.0), 'ema_residual_w': n(ks[9], (SIZE,), 1.0), 'rel_pos_bias_w': n(ks[10], (2 * MAXPOS - 1,)), 'ln_w': jnp.ones((SIZE,), jnp.float32), 'ln_b': jnp.zeros((SIZE,), jnp.float32)}
    _L0_attn_all = _L0_attn_setup()
    _L0_attn_in = {k: v for k, v in _L0_attn_all.items() if k in ('proj_v_w', 'proj_v_b', 'proj_mx_w', 'proj_mx_b', 'proj_h_w', 'proj_h_b', 'qk_weight', 'qk_bias', 'damping_factor', 'decay_factor', 'ema_expansion', 'ema_kernel_proj', 'ema_residual_w', 'rel_pos_bias_w', 'ln_w', 'ln_b')}
    del _L0_attn_all

    def _L0_ffn_setup():
        import jax, jax.numpy as jnp
        import numpy as np
        B, T, D = (4, 2048, 128)
        E, F, CAP = (8, 512, 1024)
        key = jax.random.key(seed)
        ks = jax.random.split(key, 6)
        s = 0.02
        return {'x': jax.random.normal(ks[0], (B, T, D), dtype=jnp.float32), 'Wr': jax.random.normal(ks[1], (D, E), dtype=jnp.float32) * s, 'W1': jax.random.normal(ks[2], (E, D, F), dtype=jnp.float32) * s, 'b1': jax.random.normal(ks[3], (E, F), dtype=jnp.float32) * s, 'W2': jax.random.normal(ks[4], (E, F, D), dtype=jnp.float32) * s, 'b2': jax.random.normal(ks[5], (E, D), dtype=jnp.float32) * s}
    _L0_ffn_all = _L0_ffn_setup()
    _L0_ffn_in = {k: v for k, v in _L0_ffn_all.items() if k in ('Wr', 'W1', 'b1', 'W2', 'b2')}
    del _L0_ffn_all
    return {'x': x, 'L0_tok_W': _L0_tok_in['W'], 'L0_tok_b': _L0_tok_in['b'], 'L0_tok_class_token': _L0_tok_in['class_token'], 'L0_tok_pos_embed': _L0_tok_in['pos_embed'], 'L0_attn_proj_v_w': _L0_attn_in['proj_v_w'], 'L0_attn_proj_v_b': _L0_attn_in['proj_v_b'], 'L0_attn_proj_mx_w': _L0_attn_in['proj_mx_w'], 'L0_attn_proj_mx_b': _L0_attn_in['proj_mx_b'], 'L0_attn_proj_h_w': _L0_attn_in['proj_h_w'], 'L0_attn_proj_h_b': _L0_attn_in['proj_h_b'], 'L0_attn_qk_weight': _L0_attn_in['qk_weight'], 'L0_attn_qk_bias': _L0_attn_in['qk_bias'], 'L0_attn_damping_factor': _L0_attn_in['damping_factor'], 'L0_attn_decay_factor': _L0_attn_in['decay_factor'], 'L0_attn_ema_expansion': _L0_attn_in['ema_expansion'], 'L0_attn_ema_kernel_proj': _L0_attn_in['ema_kernel_proj'], 'L0_attn_ema_residual_w': _L0_attn_in['ema_residual_w'], 'L0_attn_rel_pos_bias_w': _L0_attn_in['rel_pos_bias_w'], 'L0_attn_ln_w': _L0_attn_in['ln_w'], 'L0_attn_ln_b': _L0_attn_in['ln_b'], 'L0_ffn_Wr': _L0_ffn_in['Wr'], 'L0_ffn_W1': _L0_ffn_in['W1'], 'L0_ffn_b1': _L0_ffn_in['b1'], 'L0_ffn_W2': _L0_ffn_in['W2'], 'L0_ffn_b2': _L0_ffn_in['b2']}

def reference(x, L0_tok_W, L0_tok_b, L0_tok_class_token, L0_tok_pos_embed, L0_attn_proj_v_w, L0_attn_proj_v_b, L0_attn_proj_mx_w, L0_attn_proj_mx_b, L0_attn_proj_h_w, L0_attn_proj_h_b, L0_attn_qk_weight, L0_attn_qk_bias, L0_attn_damping_factor, L0_attn_decay_factor, L0_attn_ema_expansion, L0_attn_ema_kernel_proj, L0_attn_ema_residual_w, L0_attn_rel_pos_bias_w, L0_attn_ln_w, L0_attn_ln_b, L0_ffn_Wr, L0_ffn_W1, L0_ffn_b1, L0_ffn_W2, L0_ffn_b2):
    import jax
    import jax.numpy as jnp

    def _L0_tok_ref(X, W, b, class_token, pos_embed):
        import jax, jax.numpy as jnp
        import numpy as np
        N_PATCHES = 8
        PATCH = 28
        C = 3
        IN_D = C * PATCH * PATCH
        HID = 128
        SEQ = N_PATCHES * N_PATCHES + 1

        def _positional_embedding(seq_len, dim):
            i = np.arange(seq_len)[:, None].astype(np.float32)
            j = np.arange(dim)[None, :].astype(np.float32)
            ang = i / np.power(100000.0, j / dim)
            pe = np.where(j % 2 == 0, np.sin(ang), np.cos(ang))
            return jnp.asarray(pe, dtype=jnp.float32)
        B = X.shape[0]
        patches = X.reshape(B, C, N_PATCHES, PATCH, N_PATCHES, PATCH)
        patches = patches.transpose(0, 2, 4, 1, 3, 5).reshape(B, N_PATCHES * N_PATCHES, IN_D)
        tokens = jnp.einsum('bpi,hi->bph', patches, W) + b
        cls = jnp.broadcast_to(class_token[None, :, :], (B, 1, HID))
        tokens = jnp.concatenate([cls, tokens], axis=1)
        return tokens * pos_embed[None, :, :]

    def _L0_attn_ref(x, proj_v_w, proj_v_b, proj_mx_w, proj_mx_b, proj_h_w, proj_h_b, qk_weight, qk_bias, damping_factor, decay_factor, ema_expansion, ema_kernel_proj, ema_residual_w, rel_pos_bias_w, ln_w, ln_b):
        import jax, jax.numpy as jnp
        import numpy as np
        L, B = (512, 8)
        SIZE, NUM_HEADS, QK, V, MAXPOS = (128, 4, 128, 256, 512)
        LN_EPS = 1e-05

        def _multihead_damped_ema(x, p_raw, a_raw, beta, gamma, omega):
            length = x.shape[0]
            residual = x * omega
            xT = jnp.transpose(x, (1, 2, 0))
            p = jax.nn.sigmoid(p_raw)
            q = 1.0 - p * jax.nn.sigmoid(a_raw)
            vander = jnp.arange(length, dtype=x.dtype)[None, None, :] * jnp.log(q)
            kernel = p * beta * jnp.exp(vander)
            scaling = gamma.shape[1] ** (-0.5)
            k = jnp.einsum('dhl,dh->dl', kernel, gamma * scaling)
            n = 2 * length
            out = jnp.fft.irfft(jnp.fft.rfft(xT, n=n) * jnp.fft.rfft(k, n=n), n=n)[..., :length]
            return jax.nn.relu(jnp.transpose(out, (2, 0, 1)) + residual)

        def _simple_rel_pos_bias(w, length, max_positions):
            rel = jnp.arange(length)[None, :] - jnp.arange(length)[:, None]
            return w[max_positions - 1 + rel]
        length, batch, size = x.shape
        res_in = x
        value = jax.nn.relu(x @ proj_v_w.T + proj_v_b)
        ema_out = _multihead_damped_ema(x, damping_factor, decay_factor, ema_expansion, ema_kernel_proj, ema_residual_w)
        base = ema_out @ proj_mx_w.T + proj_mx_b
        residual_weight = jax.nn.sigmoid(base[..., :size])
        qk_gates = jax.nn.relu(base[..., size:size + QK + V])
        intermediate = base[..., size + QK + V:]
        qk = qk_gates[..., :QK]
        att_gate = qk_gates[..., QK:]
        qkp = qk[..., None, :] * qk_weight + qk_bias
        query = jnp.transpose(qkp[:, :, 0], (1, 0, 2))
        key_t = jnp.transpose(qkp[:, :, 1], (1, 0, 2))
        val_t = jnp.transpose(value, (1, 0, 2))
        bias = _simple_rel_pos_bias(rel_pos_bias_w, length, MAXPOS)
        scaling = QK ** (-0.5)
        scores = jnp.einsum('bld,bmd->blm', query * scaling, key_t) + bias
        attn = jax.nn.softmax(scores.astype(jnp.float32), axis=-1).astype(scores.dtype)
        wout = jnp.einsum('blm,bmv->blv', attn, val_t)
        wout = jnp.transpose(wout, (1, 0, 2))
        h = jax.nn.relu(intermediate + wout * att_gate @ proj_h_w.T + proj_h_b)
        out = res_in + residual_weight * (h - res_in)
        mu = out.mean(axis=-1, keepdims=True)
        var = ((out - mu) ** 2).mean(axis=-1, keepdims=True)
        out = (out - mu) * jax.lax.rsqrt(var + LN_EPS) * ln_w + ln_b
        return out

    def _L0_ffn_ref(x, Wr, W1, b1, W2, b2):
        import jax, jax.numpy as jnp
        import numpy as np
        B, T, D = (4, 2048, 128)
        E, F, CAP = (8, 512, 1024)
        Bb, Tt, Dd = x.shape
        N = Bb * Tt
        C = min(CAP, N)
        x_flat = x.reshape(N, Dd)
        logits = x_flat @ Wr
        probs = jax.nn.softmax(logits, axis=0)
        vals, idx = jax.lax.top_k(probs.T, C)
        selected = x_flat[idx]
        h = jax.nn.gelu(jnp.einsum('ecd,edf->ecf', selected, W1) + b1[:, None, :], approximate=False)
        out_e = jnp.einsum('ecf,efd->ecd', h, W2) + b2[:, None, :]
        weighted = vals[..., None] * out_e
        output = jnp.zeros_like(x_flat).at[idx.reshape(-1)].add(weighted.reshape(-1, Dd))
        return output.reshape(Bb, Tt, Dd)
    h = _L0_tok_ref(x, L0_tok_W, L0_tok_b, L0_tok_class_token, L0_tok_pos_embed)
    h = h + _L0_attn_ref(_layernorm(h, axis=-1), L0_attn_proj_v_w, L0_attn_proj_v_b, L0_attn_proj_mx_w, L0_attn_proj_mx_b, L0_attn_proj_h_w, L0_attn_proj_h_b, L0_attn_qk_weight, L0_attn_qk_bias, L0_attn_damping_factor, L0_attn_decay_factor, L0_attn_ema_expansion, L0_attn_ema_kernel_proj, L0_attn_ema_residual_w, L0_attn_rel_pos_bias_w, L0_attn_ln_w, L0_attn_ln_b)
    h = h + _L0_ffn_ref(_layernorm(h, axis=-1), L0_ffn_Wr, L0_ffn_W1, L0_ffn_b1, L0_ffn_W2, L0_ffn_b2)
    return h

_drawn_inputs = setup_inputs


def setup_inputs(seed=0):
    import zlib

    import numpy as np

    out = dict(_drawn_inputs(seed))
    spreads = {'L0_attn_proj_v_b': (0.0, 0.8),
     'L0_attn_proj_mx_b': (0.0, 0.1),
     'L0_attn_proj_h_b': (0.0, 0.1),
     'L0_attn_qk_bias': (0.0, 2.0),
     'L0_attn_ln_w': (1.0, 0.2),
     'L0_attn_ln_b': (0.0, 0.1)}
    factors = {'L0_attn_proj_v_w': 8.0,
     'L0_attn_proj_h_w': 8.0,
     'L0_attn_qk_weight': 64.0,
     'L0_attn_damping_factor': 8.0,
     'L0_attn_decay_factor': 8.0,
     'L0_attn_rel_pos_bias_w': 64.0,
     'L0_ffn_Wr': 64.0,
     'L0_ffn_W1': 64.0,
     'L0_ffn_b1': 64.0,
     'L0_ffn_W2': 64.0,
     'L0_ffn_b2': 64.0}
    for name, (base, spread) in spreads.items():
        noise = np.random.default_rng([zlib.crc32(name.encode()), seed]).standard_normal(out[name].shape)
        drawn = base * np.exp(spread * noise) if base else spread * noise
        out[name] = jnp.asarray(drawn.astype(out[name].dtype))
    for name, factor in factors.items():
        out[name] = (out[name] * factor).astype(out[name].dtype)
    return out
```

```python
import concourse.bass as bass
from concourse import mybir
from contextlib import ExitStack


class Count:

    def __init__(self, sem, per=1):
        self.sem = sem
        self.per = per

    def done(self, n, k=None):
        return self.sem, n * self.per + (self.per if k is None else k)


def begun(n):
    return not isinstance(n, int) or n >= 0


class Group:

    def __init__(self, row, g, u, tiles, position, parity, stored):
        self.row = row
        self.g = g
        self.u = u
        self.tiles = tiles
        self.position = position
        self.parity = parity
        self.stored = stored
        self.cols = tiles * 128


def vit_tower(nc, x, tok_w, tok_b, cls_token, pos_embed, proj_v_w, proj_v_b, proj_mx_w, proj_mx_b,
              proj_h_w, proj_h_b, qk_weight, qk_bias, damping, decay, ema_expansion, ema_proj,
              ema_residual, rel_pos_w, ln_w, ln_b, router_w, w1, b1, w2, b2, out):
    F32 = mybir.dt.float32
    BF16 = mybir.dt.bfloat16
    I32 = mybir.dt.int32
    ALU = mybir.AluOpType
    ACT = mybir.ActivationFunctionType
    AX = mybir.AxisListType
    ds = bass.ds

    B, C, IMG, _ = x.shape
    SEQ, D = pos_embed.shape
    NP = 8
    PATCH = IMG // NP
    V = proj_v_w.shape[0]
    VC = V // 128
    QK = qk_weight.shape[1]
    HEADS = damping.shape[1]
    MAXPOS = (rel_pos_w.shape[0] + 1) // 2
    E, _, FF = w1.shape
    FC = FF // 128
    CAP = 1024
    NTOK = B * SEQ
    EPS = 1e-5
    QSCALE = QK ** -0.5
    EMA_SCALE = HEADS ** -0.5
    ROW = D + E

    PASSES = (PATCH * C) // 4
    REST = PATCH - PASSES
    KROWS = 96 + PATCH
    HALF = B // 2
    SLAB = HALF * IMG
    NCOL = HALF * NP

    ctx = ExitStack()
    with ctx:
        def sb(name, shape, dt=F32):
            return ctx.enter_context(nc.sbuf_tensor(name, shape, dt))

        def count(name, per=1):
            return Count(ctx.enter_context(nc.semaphore(name)), per)

        XS = sb("XS", [128, 2, SLAB])
        WT = sb("WT", [128, PASSES, D])
        ident = sb("ident", [128, 128])
        VT = sb("VT", [128, 120])
        WvT = sb("WvT", [128, V])
        WmT = sb("WmT", [128, 5, 128])
        WhT = sb("WhT", [128, VC, D])
        Wr = sb("Wr", [128, E])
        relb = sb("relb", [128, 128])
        nbv = sb("nbv", [128, V])
        lnw = sb("lnw", [128, D])
        lnb = sb("lnb", [128, D])
        qdec = sb("qdec", [128, HEADS, 4 * 128])
        ema_in = sb("ema_in", [128, 4, HEADS])
        ema_t = sb("ema_t", [128, 4, HEADS])
        ema_c = sb("ema_c", [128, HEADS])
        derived = sb("derived", [128, 4])
        neghalf = sb("neghalf", [128, 4])
        LG = sb("LG", [128, E, SEQ])
        tokT = sb("tokT", [128, NP, B])
        H = sb("H", [128, 2, 4, D])
        X = sb("X", [128, 4, D])
        XT = sb("XT", [128, 2, 512])
        Vv = sb("Vv", [128, 2, 4, V])
        Y = sb("Y", [128, 2, 512])
        ET = sb("ET", [128, 2, 512])
        QKT = sb("QKT", [128, 512])
        QT = sb("QT", [128, 512])
        GT = sb("GT", [128, 2, VC, 512])
        TH = sb("TH", [128, 2, 512])
        S = sb("S", [128, 2, 4, 128])
        PT = sb("PT", [128, 512])
        G = sb("G", [128, VC, 512])
        HR = sb("HR", [128, 512])
        OT = X[:, :, :].rearrange("p t n -> p (t n)")
        O = sb("O", [128, 2, 4, D])
        XR = sb("XR", [128, 2, 4, ROW])
        X2T = X
        stats = sb("stats", [128, 4, 6])
        mvA = sb("mvA", [128, 2, 4, 2])
        mvB = sb("mvB", [128, 2, 4, 2])
        mvC = sb("mvC", [128, 2, 4, 2])
        rsA = sb("rsA", [128, 2, 4])
        rsB = sb("rsB", [128, 2, 4])
        rsC = sb("rsC", [128, 2, 4])
        nmax = sb("nmax", [128, 2, 4])
        ssum = sb("ssum", [128, 2, 4])
        rsum = sb("rsum", [128, 2, 4])

        slab1 = XS[:, 1, :]
        WN = slab1[:, 0:C * PATCH * PATCH]
        WP = slab1[:, 2352:2352 + PASSES * 128].rearrange("p (t k) -> p t k", t=PASSES)
        at = 2352 + PASSES * 128
        WvN = slab1[:, at:at + V].rearrange("p (k d) -> p k d", k=VC)
        WmN = slab1[:, at + V:at + V + 640].rearrange("p (k d) -> p k d", k=5)
        WhN = slab1[:, at + V + 640:at + V + 640 + V]
        VN = slab1[:, at + 2 * V + 640:at + 2 * V + 640 + D]
        relN = slab1[:, at + 2 * V + 640 + D:at + 2 * V + 640 + 2 * D]
        flip = slab1[:, at + 2 * V + 640 + 2 * D:at + 2 * V + 640 + 3 * D]
        zeros = LG[:, :, :].rearrange("p e s -> p (e s)")[:, 0:448]

        R_TOKB, R_BV, R_BMX, R_BH, R_QKW, R_QKB, R_OMEGA, R_B1, R_B2, R_POS, R_CLS = \
            0, 1, 3, 8, 9, 11, 13, 14, 46, 54, 119

        def vcol(n):
            return VT[:, n:n + 1]

        flat = XS[:, :, :].rearrange("p a b -> p (a b)")
        spot = [0]

        def view(cols, dt=F32):
            a = spot[0]
            words = cols if dt != BF16 else (cols + 1) // 2
            spot[0] += words
            v = flat[:, a:a + words]
            return v if dt == F32 else v.bitcast(dt)

        W1s = view(2 * FF).rearrange("p (a f) -> p a f", a=2)
        W2s = view(2 * FF).rearrange("p (a c d) -> p a c d", a=2, c=FC)
        R = view(520)
        Dm = view(520)
        junk = view(520)
        EX = view(520)
        S1 = view(520)
        EQ = view(520)
        CE = view(520)
        SLR = view(520)
        SL = view(E * SEQ).rearrange("p (e s) -> p e s", e=E)
        SLi = view(E * SEQ, I32)
        HIi = view(E * SEQ, I32)
        LOi = view(E * SEQ, I32)
        HI = view((E + 1) * SEQ + 1, BF16)[:, 0:(E + 1) * SEQ].rearrange("p (e s) -> p e s", s=SEQ)
        LO = view((E + 1) * SEQ + 1, BF16)[:, 0:(E + 1) * SEQ].rearrange("p (e s) -> p e s", s=SEQ)
        OHh = view(SEQ * 32, BF16).rearrange("p (s h) -> p s h", h=32)
        OHl = view(SEQ * 32, BF16).rearrange("p (s h) -> p s h", h=32)
        OHn = view(SEQ * 64, BF16).rearrange("p (s t h) -> p s t h", t=2, h=32)
        io32 = view(32, BF16)
        ioP = view(66, BF16)
        iob = view(1)
        IX = view(32, I32)
        IXf = view(64)
        IDX = view(2 * 8, I32).rearrange("p (a k) -> p a k", a=2)
        IDXs = view(2 * 8, I32).rearrange("p (a k) -> p a k", a=2)
        XG = view(2 * 8 * ROW).rearrange("p (a k r) -> p a k r", a=2, k=8)
        XGT = view(2 * 512).rearrange("p (a n) -> p a n", a=2)
        HT = view(2 * FC * 512).rearrange("p (a f n) -> p a f n", a=2, f=FC)
        YT = view(2 * 512).rearrange("p (a n) -> p a n", a=2)
        OW = view(2 * 8 * D).rearrange("p (a k d) -> p a k d", a=2, k=8)
        blk = view(128)
        ones = view(128)
        low = view(128)
        sel0 = view(E)
        econst = view(8)
        vdiff = view(2 * 8).rearrange("p (a k) -> p a k", a=2)
        vexp = view(2 * 8).rearrange("p (a k) -> p a k", a=2)
        val = view(2 * 8).rearrange("p (a k) -> p a k", a=2)
        small = view(32)
        smalli = view(8, I32)
        mrow = view(128)
        MB = view(E)
        IS = view(E)
        msel = view(2 * E)
        assert spot[0] <= 2 * SLAB

        bank = [ctx.enter_context(nc.psum_tensor(f"bank{n}", [128, 512], F32)) for n in range(8)]
        TOK = [bank[0], bank[1]]
        TB0, TB1 = bank[2], bank[3]
        VB = [bank[4], bank[5]]
        DB0, DB1 = bank[6], bank[7]

        rows_d = nc.dram_tensor("token_rows", [NTOK, ROW], F32, kind="Internal").ap()
        lg_d = nc.dram_tensor("logits_scratch", [B, E, SEQ], F32, kind="Internal").ap()
        slot_d = nc.dram_tensor("slot_scratch", [E, NTOK], F32, kind="Internal").ap()
        idx_d = nc.dram_tensor("index_scratch", [E, CAP], I32, kind="Internal").ap()
        rows_v = rows_d.rearrange("(b s) r -> b s r", s=SEQ)
        out_flat = out.rearrange("b s d -> (b s) d")

        w_loaded = count("w_loaded", 16)
        v_loaded = count("v_loaded", 16 * 11)
        m_loaded = count("m_loaded", 16 * 3)
        c_loaded = count("c_loaded", 16 * 9)
        zero_ready = count("zero_ready")
        gaps_done = count("gaps_done", 16 * 6)
        const_ready = count("const_ready")
        pool_c = count("pool_c")
        wp_ready = count("wp_ready")
        pe_pro = count("pe_pro")
        pro_evac = count("pro_evac")
        pro_sig = count("pro_sig")
        dve_pro = count("dve_pro")
        consts_done = count("consts_done")
        load = [count(f"load{h}", 48) for h in range(2)]
        pack = [count(f"pack{h}", C) for h in range(2)]
        pe_tok = [count(f"pe_tok{h}") for h in range(2)]
        dve_K = [count(f"dve_K{h}") for h in range(2)]
        pe_T, act_T, dve_T = count("pe_T"), count("act_T"), count("dve_T", 2)
        pool_N, dve_N = count("pool_N", 2), count("dve_N")
        pe_X, act_X = count("pe_X"), count("act_X")
        pe_V, dve_V = count("pe_V", 2), count("dve_V", 2)
        act_E, dve_E, relu_E = count("act_E"), count("dve_E", 8), count("relu_E")
        pe_D, act_D, pool_D = count("pe_D", 4), count("act_D", 4), count("pool_D", 2)
        pe_S, dve_S, act_S = count("pe_S"), count("dve_S", 2), count("act_S")
        dve_Z = count("dve_Z", 2)
        pe_P, act_P = count("pe_P"), count("act_P")
        pe_O, dve_O = count("pe_O", 2), count("dve_O", 2)
        pe_H, act_H, pool_H, dve_H = count("pe_H"), count("act_H"), count("pool_H"), count("dve_H", 2)
        pe_L, act_L, dve_L = count("pe_L"), count("act_L"), count("dve_L", 2)
        pool_B, pool_L = count("pool_B"), count("pool_L", 2)
        dve_M, pool_M = count("dve_M", 5), count("pool_M", 2)
        dve_Q, pe_Q, act_Q = count("dve_Q"), count("pe_Q"), count("act_Q")
        pe_R, act_R = count("pe_R"), count("act_R", 2)
        out_stored = [count(f"out_stored{h}", 16) for h in range(2)]
        row_stored = [count(f"row_stored{h}", 16) for h in range(2)]

        passed = count("passed")
        passed_sp = count("passed_sp")

        ffn_consts = count("ffn_consts")
        lg_out = count("lg_out", 16)
        r_in = count("r_in", 16 * E)
        dve_f = count("dve_f")
        pe_f = count("pe_f")
        act_f = count("act_f")
        cnt_ready, cnt_summed, step_done = count("cnt_ready"), count("cnt_summed"), count("step_done", 4)
        slr_ready = count("slr_ready")
        sl_out, sl_in = count("sl_out", 16), count("sl_in", 16)
        hilo = count("hilo")
        bcast_ready = count("bcast_ready")
        oh_h, oh_l, oh_b, oh_p = count("oh_h"), count("oh_l"), count("oh_b"), count("oh_p")
        pe_C, dve_C = count("pe_C"), count("dve_C", 2)
        ix_out, ix_in = count("ix_out", 16), count("ix_in", 16)
        w_in = [count(f"w_in{h}", 32) for h in range(2)]
        gathered = [count(f"gathered{h}", 16 * 8) for h in range(2)]
        scattered = count("scattered", 16 * 8)
        kept = count("kept")
        val_d, val_p, val_r = count("val_d"), count("val_p"), count("val_r")
        pe_gt, act_gt = count("pe_gt"), count("act_gt")
        pe_hid, act_hid = count("pe_hid", FC), count("act_hid", FC)
        pe_y, dve_y = count("pe_y"), count("dve_y")
        pe_yt, dve_ow = count("pe_yt"), count("dve_ow")

        emptied = {"T": act_T, "P": act_P, "Q": act_Q, "X": act_X, "L": act_L, "R": act_R,
                   "H": act_H}
        before = {
            "T": {0: ("Q", -1), 1: ("T", -1), None: None},
            "P": {0: ("T", 1), 1: ("P", -1), None: ("T", 0)},
            "Q": {0: ("P", 1), 1: ("Q", -1), None: ("P", 0)},
            "X": {0: ("R", -1), 1: ("X", -1), None: None},
            "L": {0: ("X", 1), 1: ("L", -1), None: ("X", 0)},
            "R": {0: ("L", 1), 1: ("R", -1), None: ("L", 0)},
        }

        def bank_free(eng, stage, gr):
            user = before[stage][gr.u]
            if user:
                eng.wait_ge(*emptied[user[0]].done(gr.g + user[1]))

        CLS = Group(None, 0, None, 1, 0, 0, 0)

        def groups(i):
            return (Group(i - 1, 2 * i - 1, 0, 4, 8 * i - 7, 1, i - 1), Group(i - 1, 2 * i, 1, 4, 8 * i - 3, 0, i))

        ORDER = [("T", 0), ("T", 1), ("N", 0), ("N", 1), ("X", 0), ("X", 1), ("V", 0), ("E", 0), ("V", 1),
                 ("E", 1), ("D", 0), ("G", 1, 0), ("S", 0), ("D", 1), ("G", 1, 1), ("S", 1), ("Z", 0),
                 ("P", 0), ("G", 1, 2), ("Z", 1), ("P", 1), ("O", 0), ("O", 1), ("K", 0), ("H", 0), ("H", 1),
                 ("L", 0), ("L", 1), ("M", 0), ("M", 1), ("Q", 0), ("G", 0, 0), ("Q", 1), ("R", 0),
                 ("G", 0, 1), ("R", 1), ("G", 0, 2), ("K", 1)]
        CLS_ORDER = [("T",), ("N",), ("X",), ("G", 1, 0), ("V",), ("E",), ("G", 1, 1), ("D",), ("S",), ("G", 1, 2),
                     ("Z",), ("P",), ("O",), ("K", 0), ("H",), ("L",), ("G", 0, 0), ("M",), ("Q",), ("G", 0, 1),
                     ("R",), ("G", 0, 2), ("K", 1)]

        def schedule(i, attention, tokens, more):
            keep = []
            for s, *w in CLS_ORDER if attention == "cls" else ORDER:
                if s == "K":
                    if tokens:
                        keep.append((s, (w[0], i)))
                elif s == "G":
                    if tokens if w[0] else more:
                        keep.append((s, (w[0], w[1], i if w[0] else i + 1)))
                else:
                    keep.append((s, (groups(i)[w[0]] if w else CLS,)))
            return keep

        block = ctx.enter_context(nc.Block())

        def run(eng, stages, tokens_at=None):
            def iteration(i, attention, tokens, more):
                for s, w in schedule(i, attention, tokens, more):
                    if s in stages:
                        stages[s](*w)
                    if tokens_at and tokens and s not in "KG":
                        tokens_at(s, w[0], i)
            iteration(0, "cls", True, True)
            iteration(1, "groups", True, True)
            with eng.Fori(2, NP - 1) as i:
                iteration(i, "groups", True, True)
            iteration(NP - 1, "groups", True, False)
            iteration(NP, "groups", False, False)

        @block.sync
        def _(sp):
            def load_slab(half, hy):
                for c in range(C):
                    sp.dma_start(
                        XS[32 * c:32 * c + PATCH, half, :].rearrange("p (b w) -> p b w", b=HALF),
                        x[HALF * half:HALF * half + HALF, c, ds(hy * PATCH, PATCH), :].rearrange("b p w -> p b w")
                    ).then_inc(load[half].sem, 16)

            def gap_rows(half):
                for c in range(C):
                    sp.dma_start(
                        XS[32 * c + PATCH:32 * c + 32, half, :].rearrange("p (a z) -> p a z", z=448),
                        zeros[0:4, :].unsqueeze(1).to_broadcast([4, SLAB // 448, 448])
                    ).then_inc(gaps_done.sem, 16)

            sp.dma_start(WN, tok_w).then_inc(w_loaded.sem, 16)
            load_slab(0, 0)
            sp.wait_ge(*zero_ready.done(0))
            gap_rows(0)
            sp.wait_ge(*pe_pro.done(8))
            load_slab(1, 0)
            gap_rows(1)

            def store(gr):
                sp.wait_ge(*dve_M.done(gr.g, 3))
                sp.dma_start(out[:, ds(gr.position, gr.tiles), :], O[:, gr.parity, 0:gr.tiles, :])\
                    .then_inc(out_stored[gr.parity].sem, 16)
                sp.wait_ge(*act_R.done(gr.g))
                sp.sem_inc(passed_sp.sem, 1)
                sp.dma_start(rows_v[:, ds(gr.position, gr.tiles), :], XR[:, gr.parity, 0:gr.tiles, :])\
                    .then_inc(row_stored[gr.parity].sem, 16)

            def iteration(i, gs, more):
                if more:
                    sp.wait_ge(*pe_tok[0].done(i))
                    load_slab(0, i + 1)
                for gr in gs:
                    store(gr)
                if more:
                    sp.wait_ge(*pe_tok[1].done(i))
                    load_slab(1, i + 1)

            iteration(0, [CLS], True)
            iteration(1, groups(1), True)
            with sp.Fori(2, NP - 1) as i:
                iteration(i, groups(i), True)
            iteration(NP - 1, groups(NP - 1), False)

            def load_experts(h, e):
                sp.dma_start(W1s[:, h, :], w1[ds(e, 1), :, :].rearrange("e d f -> d (e f)")).then_inc(w_in[h].sem, 16)
                sp.dma_start(W2s[:, h, :, :], w2[ds(e, 1), :, :].rearrange("e (c f) d -> f (e c) d", f=128))\
                    .then_inc(w_in[h].sem, 16)

            sp.wait_ge(*pe_tok[0].done(NP - 1))
            sp.wait_ge(*pe_tok[1].done(NP - 1))
            for h in range(2):
                load_experts(h, h)
            for gr in groups(NP):
                store(gr)

            sp.wait_ge(*act_R.done(2 * NP))
            sp.dma_start(lg_d, LG[:, :, :]).then_inc(lg_out.sem, 16)
            sp.wait_ge(*lg_out.done(0))
            for e in range(E):
                sp.dma_start(R[16 * e:16 * e + 16, :].rearrange("c (b s) -> c b s", s=SEQ),
                             lg_d[:, e, :].rearrange("(c b) s -> c b s", c=16)).then_inc(r_in.sem, 16)
            sp.wait_ge(*slr_ready.done(0))
            sp.dma_start(slot_d.rearrange("e (c n) -> (e c) n", c=16), SLR).then_inc(sl_out.sem, 16)
            sp.wait_ge(*sl_out.done(0))
            sp.dma_start(SL, slot_d.rearrange("e (b s) -> b e s", s=SEQ)).then_inc(sl_in.sem, 16)

            def indices(e, h):
                sp.wait_ge(*dve_C.done(e))
                sp.dma_start(idx_d[ds(e, 1), :].rearrange("e (h l) -> (e h) l", l=32), IX[0:32, :])\
                    .then_inc(ix_out.sem, 16)
                sp.wait_ge(*ix_out.done(e))
                sp.sem_inc(passed_sp.sem, 1)
                if begun(e - 2):
                    sp.wait_ge(*kept.done(e - 2))
                sp.dma_start(IDX[:, h, :], idx_d[ds(e, 1), :].rearrange("e (q k) -> (e q) k", k=8))\
                    .then_inc(ix_in.sem, 16)

            def expert(e, h, lists, load):
                if lists:
                    indices(e + 2, h)
                if load:
                    if begun(2 * e - 1):
                        sp.wait_ge(*pe_y.done(2 * e - 1))
                    load_experts(1 - h, e + 1)

            indices(0, 0)
            indices(1, 1)
            expert(0, 0, True, False)
            expert(1, 1, True, True)
            with sp.Fori(1, E // 2 - 1) as j:
                expert(2 * j, 0, True, True)
                expert(2 * j + 1, 1, True, True)
            expert(E - 2, 0, False, True)
            sp.wait_ge(*out_stored[0].done(NP))
            sp.wait_ge(*out_stored[1].done(NP - 1))
            sp.wait_ge(*row_stored[0].done(NP))
            sp.wait_ge(*row_stored[1].done(NP - 1))

        @block.gpsimd
        def _(pool):
            pool.memset(zeros, 0.0).then_inc(zero_ready.sem, 1)
            pool.memset(ident[:, :], 0.0)
            pool.memset(flip, 0.0)
            pool.memset(neghalf[:, :], -0.5).then_inc(pool_c.sem, 1)
            pool.wait_ge(*pool_c.done(0))
            pool.affine_select(out=ident[:, :], in_=ident[:, :], compare_op=ALU.not_equal, fill=1.0, base=0,
                               pattern=[[-1, 128]], channel_multiplier=1)
            pool.affine_select(out=flip, in_=flip, compare_op=ALU.not_equal, fill=1.0, base=-127,
                               pattern=[[1, 128]], channel_multiplier=1).then_inc(const_ready.sem, 1)

            def rstd(done, per, mv, rs, gr):
                p, n = gr.parity, gr.tiles
                pool.tensor_scalar(rs[:, p, 0:n], mv[:, p, 0:n, 1], EPS, None, ALU.add).then_inc(done.sem, 1)
                pool.wait_ge(*done.done(gr.g, 1))
                pool.tensor_tensor(rs[:, p, 0:n], rs[:, p, 0:n], neghalf[:, 0:n], ALU.pow).then_inc(done.sem, 1)

            def stage_N(gr):
                pool.wait_ge(*dve_T.done(gr.g))
                pool.sem_inc(passed.sem, 1)
                rstd(pool_N, 2, mvA, rsA, gr)

            def stage_X(gr):
                pool.wait_ge(*dve_N.done(gr.g))
                h = H[:, gr.parity, 0:gr.tiles, :]
                pool.tensor_tensor(h, h, lnb[:, :].unsqueeze(1).to_broadcast([128, gr.tiles, D]), ALU.add)\
                    .then_inc(pool_B.sem, 1)

            def stage_D(gr):
                n = gr.cols
                pool.wait_ge(*act_D.done(gr.g, 1))
                if begun(gr.g - 1):
                    pool.wait_ge(*pe_S.done(gr.g - 1))
                    pool.sem_inc(passed.sem, 1)
                pool.tensor_scalar(QT[:, 0:n], QKT[:, 0:n], derived[:, 0:1], derived[:, 1:2], ALU.mult, ALU.add)\
                    .then_inc(pool_D.sem, 1)
                pool.tensor_scalar(QKT[:, 0:n], QKT[:, 0:n], vcol(R_QKW + 1), vcol(R_QKB + 1), ALU.mult, ALU.add)\
                    .then_inc(pool_D.sem, 1)

            def stage_H(gr):
                n = gr.cols
                pool.wait_ge(*act_H.done(gr.g))
                pool.tensor_tensor(HR[:, 0:n], HR[:, 0:n], XT[:, gr.parity, 0:n], ALU.subtract)\
                    .then_inc(pool_H.sem, 1)

            def stage_L(gr):
                pool.wait_ge(*dve_L.done(gr.g))
                pool.sem_inc(passed.sem, 1)
                rstd(pool_L, 2, mvB, rsB, gr)

            def stage_M(gr):
                pool.wait_ge(*dve_M.done(gr.g))
                pool.sem_inc(passed.sem, 1)
                rstd(pool_M, 2, mvC, rsC, gr)

            pool.wait_ge(*consts_done.done(0))
            run(pool, {"N": stage_N, "X": stage_X, "D": stage_D, "H": stage_H, "L": stage_L, "M": stage_M})

            pool.wait_ge(*pe_tok[1].done(NP - 1))
            pool.wait_ge(*pe_tok[0].done(NP - 1))
            pool.memset(blk, 1.0)
            pool.memset(ones, 1.0)
            pool.memset(sel0, 0.0)
            pool.memset(econst, 2.718281828459045)
            pool.iota(io32, pattern=[[1, 32]], base=0, channel_multiplier=0, allow_small_or_imprecise_dtypes=True)
            pool.iota(ioP[:, 0:SEQ], pattern=[[1, SEQ]], base=0, channel_multiplier=0,
                      allow_small_or_imprecise_dtypes=True)
            pool.iota(iob, pattern=[[0, 1]], base=0, channel_multiplier=1, allow_small_or_imprecise_dtypes=True)\
                .then_inc(pool_c.sem, 1)
            pool.wait_ge(*pool_c.done(1))
            blk3 = blk.rearrange("p (e c) -> p e c", e=E)
            pool.affine_select(out=blk3, in_=blk3, compare_op=ALU.is_ge, fill=0.0, base=0,
                               pattern=[[-16, E], [0, 16]], channel_multiplier=1).then_inc(pool_c.sem, 1)
            pool.wait_ge(*pool_c.done(2))
            pool.affine_select(out=blk3, in_=blk3, compare_op=ALU.is_ge, fill=0.0, base=15,
                               pattern=[[16, E], [0, 16]], channel_multiplier=-1).then_inc(pool_c.sem, 1)
            pool.wait_ge(*pool_c.done(3))
            pool.affine_select(out=low, in_=blk, compare_op=ALU.is_gt, fill=0.0, base=0,
                               pattern=[[1, 128]], channel_multiplier=-1)
            pool.affine_select(out=sel0, in_=sel0, compare_op=ALU.not_equal, fill=1.0, base=0,
                               pattern=[[-16, E]], channel_multiplier=1).then_inc(ffn_consts.sem, 1)

            def gather(e, h):
                pool.wait_ge(*ix_in.done(e))
                pool.sem_inc(passed.sem, 1)
                for k in range(8):
                    pool.indirect_dma_start(out=XG[:, h, k, :], out_offset=None, in_=rows_d,
                                            in_offset=bass.IndirectOffsetOnAxis(ap=IDX[:, h, k:k + 1], axis=0))\
                        .then_inc(gathered[h].sem, 16)

            def weights(e, h):
                pool.wait_ge(*val_d.done(e))
                pool.tensor_tensor(vexp[:, h, :], econst, vdiff[:, h, :], ALU.pow).then_inc(val_p.sem, 1)

            def keep(e, h):
                pool.tensor_copy(IDXs[:, h, :], IDX[:, h, :]).then_inc(kept.sem, 1)
                pool.wait_ge(*kept.done(e))
                pool.sem_inc(passed.sem, 1)

            def scatter(e, h):
                for k in range(8):
                    if k % 4 == 0:
                        pool.wait_ge(*dve_ow.done(2 * e + k // 4))
                        pool.sem_inc(passed.sem, 1)
                    pool.indirect_dma_start(out=out_flat, in_=OW[:, h, k, :], in_offset=None,
                                            out_offset=bass.IndirectOffsetOnAxis(ap=IDXs[:, h, k:k + 1], axis=0),
                                            compute_op=ALU.add).then_inc(scattered.sem, 16)

            def expert(e, h, before, lists, last=False):
                if before:
                    if begun(e - 2):
                        pool.wait_ge(*scattered.done(e - 2))
                        pool.sem_inc(passed.sem, 1)
                keep(e, h)
                if lists:
                    pool.wait_ge(*pe_gt.done(2 * e + 1))
                    pool.sem_inc(passed.sem, 1)
                    gather(e + 2, h)
                if before:
                    scatter(e - 1, 1 - h)
                if not last:
                    weights(e + 1, 1 - h)

            pool.wait_ge(*row_stored[0].done(NP))
            pool.wait_ge(*row_stored[1].done(NP - 1))
            pool.wait_ge(*out_stored[0].done(NP))
            pool.wait_ge(*out_stored[1].done(NP - 1))
            gather(0, 0)
            gather(1, 1)
            weights(0, 0)
            expert(0, 0, False, True)
            expert(1, 1, True, True)
            with pool.Fori(1, E // 2 - 1) as j:
                expert(2 * j, 0, True, True)
                expert(2 * j + 1, 1, True, True)
            expert(E - 2, 0, True, False)
            expert(E - 1, 1, True, False, last=True)
            pool.wait_ge(*scattered.done(E - 2))
            scatter(E - 1, 1)
            pool.wait_ge(*scattered.done(E - 1))

        @block.scalar
        def _(act):
            vectors = [(tok_b, R_TOKB, 1), (proj_v_b, R_BV, VC), (proj_mx_b, R_BMX, 5), (proj_h_b, R_BH, 1),
                       (qk_weight, R_QKW, 2), (qk_bias, R_QKB, 2), (ema_residual, R_OMEGA, 1),
                       (b1, R_B1, E * FC), (b2, R_B2, E), (pos_embed, R_POS, SEQ), (cls_token, R_CLS, 1)]
            for v, row, n in vectors:
                src = v.rearrange("(a n) -> a n", n=128) if len(v.shape) == 1 else \
                    v.rearrange("a (k n) -> (a k) n", n=128)
                act.dma_start(VN[row:row + n, :], src).then_inc(v_loaded.sem, 16)
            act.dma_start(WvN, proj_v_w.rearrange("(k p) d -> p k d", p=128)).then_inc(m_loaded.sem, 16)
            act.dma_start(WmN, proj_mx_w.rearrange("(k p) d -> p k d", p=128)).then_inc(m_loaded.sem, 16)
            act.dma_start(WhN, proj_h_w).then_inc(m_loaded.sem, 16)
            for n, v in enumerate((damping, decay, ema_expansion)):
                act.dma_start(ema_in[:, n, :], v.rearrange("d h o -> d (h o)")).then_inc(c_loaded.sem, 16)
            act.dma_start(ema_in[:, 3, :], ema_proj).then_inc(c_loaded.sem, 16)
            act.dma_start(Wr[:, :], router_w).then_inc(c_loaded.sem, 16)
            act.dma_start(relN, bass.AP(rel_pos_w.tensor, MAXPOS - 128, [[1, 128], [1, 128]]))\
                .then_inc(c_loaded.sem, 16)
            act.dma_start(nbv[:, :], bass.AP(proj_v_b.tensor, 0, [[0, 128], [1, V]])).then_inc(c_loaded.sem, 16)
            act.dma_start(lnw[:, :], bass.AP(ln_w.tensor, 0, [[0, 128], [1, D]])).then_inc(c_loaded.sem, 16)
            act.dma_start(lnb[:, :], bass.AP(ln_b.tensor, 0, [[0, 128], [1, D]])).then_inc(c_loaded.sem, 16)

            act.wait_ge(*c_loaded.done(0))
            act.activation(ema_t[:, 0:2, :], ema_in[:, 0:2, :], ACT.Exp, scale=-1.0).then_inc(pro_sig.sem, 1)
            wt = WT[:, :, :].rearrange("p t k -> p (t k)")
            evacs = [(VT[:, :], bank[5][:, 0:120]), (WvT[:, :], bank[5][:, 128:384]),
                     (WmT[:, 0:4, :].rearrange("p k d -> p (k d)"), bank[6][:, :]),
                     (WmT[:, 4, :], bank[7][:, 0:128]),
                     (WhT[:, :, :].rearrange("p k d -> p (k d)"), bank[7][:, 128:384]),
                     (relb[:, :], bank[7][:, 384:512])]
            waits = [0, 0, 1, 2, 2, 2]
            for (dst, src), w in zip(evacs, waits):
                act.wait_ge(*pe_pro.done(w))
                act.activation(dst, src, ACT.Copy).then_inc(pro_evac.sem, 1)
            for n in range(5):
                act.wait_ge(*pe_pro.done(3 + n))
                act.activation(wt[0:KROWS, 512 * n:512 * n + 512], bank[n][0:KROWS, :], ACT.Copy)\
                    .then_inc(pro_evac.sem, 1)
            act.wait_ge(*pe_pro.done(8))
            act.activation(wt[0:KROWS, 2560:2688], bank[5][0:KROWS, 384:512], ACT.Copy).then_inc(pro_evac.sem, 1)
            act.wait_ge(*consts_done.done(0))
            act.wait_ge(*gaps_done.done(0))

            def copy(dst, src, done):
                act.activation(dst, src, ACT.Copy).then_inc(done.sem, 1)

            def tiles(t, gr):
                return t[:, gr.parity, 0:gr.tiles, :]

            def ps3(b, gr):
                return b[:, 0:gr.cols].rearrange("p (t n) -> p t n", n=128)

            def stage_T(gr):
                act.wait_ge(*pe_T.done(gr.g))
                if begun(gr.g - 2):
                    act.wait_ge(*pool_B.done(gr.g - 2))
                if begun(gr.g - 2):
                    act.wait_ge(*dve_M.done(gr.g - 2))
                copy(tiles(H, gr), ps3(TB0, gr), act_T)

            def stage_X(gr):
                act.wait_ge(*pe_X.done(gr.g))
                if begun(gr.g - 2):
                    act.wait_ge(*dve_H.done(gr.g - 2))
                copy(XT[:, gr.parity, 0:gr.cols], TB1[:, 0:gr.cols], act_X)

            def stage_E(gr):
                n, p = gr.cols, gr.parity
                act.wait_ge(*act_X.done(gr.g))
                if begun(gr.g - 2):
                    act.wait_ge(*pe_H.done(gr.g - 2))
                act.activation(ET[:, p, 0:n], XT[:, p, 0:n], ACT.Copy, scale=vcol(R_OMEGA)).then_inc(act_E.sem, 1)
                act.wait_ge(*dve_E.done(gr.g))
                act.activation(ET[:, p, 0:n], ET[:, p, 0:n], ACT.Relu).then_inc(relu_E.sem, 1)

            def stage_D(gr):
                n, p = gr.cols, gr.parity
                act.wait_ge(*pe_D.done(gr.g, 1))
                if begun(gr.g - 1):
                    act.wait_ge(*pe_S.done(gr.g - 1))
                act.activation(QKT[:, 0:n], DB0[:, 0:n], ACT.Relu, bias=vcol(R_BMX + 1)).then_inc(act_D.sem, 1)
                act.wait_ge(*pe_D.done(gr.g, 2))
                if begun(gr.g - 2):
                    act.wait_ge(*dve_O.done(gr.g - 2))
                act.activation(GT[:, p, 0, 0:n], DB1[:, 0:n], ACT.Relu, bias=vcol(R_BMX + 2)).then_inc(act_D.sem, 1)
                act.wait_ge(*pe_D.done(gr.g, 3))
                act.activation(GT[:, p, 1, 0:n], DB0[:, 0:n], ACT.Relu, bias=vcol(R_BMX + 3)).then_inc(act_D.sem, 1)
                act.wait_ge(*pe_D.done(gr.g, 4))
                if begun(gr.g - 2):
                    act.wait_ge(*dve_H.done(gr.g - 2))
                act.activation(TH[:, p, 0:n], DB1[:, 0:n], ACT.Tanh, bias=derived[:, 3:4], scale=0.5)\
                    .then_inc(act_D.sem, 1)

            def stage_S(gr):
                p = gr.parity
                act.wait_ge(*dve_S.done(gr.g))
                if begun(gr.g - 2):
                    act.wait_ge(*dve_Z.done(gr.g - 2, 2))
                for t in range(gr.tiles):
                    last = act.activation(S[:, p, t, :], S[:, p, t, :], ACT.Exp, bias=nmax[:, p, t:t + 1],
                                          accum_out=ssum[:, p, t:t + 1])
                last.then_inc(act_S.sem, 1)

            def stage_P(gr):
                act.wait_ge(*pe_P.done(gr.g))
                if begun(gr.g - 1):
                    act.wait_ge(*pe_O.done(gr.g - 1))
                copy(PT[:, 0:gr.cols], TB0[:, 0:gr.cols], act_P)

            def stage_H(gr):
                n = gr.cols
                act.wait_ge(*pe_H.done(gr.g))
                if begun(gr.g - 1):
                    act.wait_ge(*dve_H.done(gr.g - 1))
                act.activation(HR[:, 0:n], DB1[:, 0:n], ACT.Relu, bias=derived[:, 2:3]).then_inc(act_H.sem, 1)

            def stage_L(gr):
                act.wait_ge(*pe_L.done(gr.g))
                if begun(gr.stored - 1):
                    act.wait_ge(*out_stored[gr.parity].done(gr.stored - 1))
                if begun(gr.g - 2):
                    act.wait_ge(*dve_Q.done(gr.g - 2))
                copy(tiles(O, gr), ps3(TB1, gr), act_L)

            def stage_Q(gr):
                act.wait_ge(*pe_Q.done(gr.g))
                if begun(gr.g - 1):
                    act.wait_ge(*pe_R.done(gr.g - 1))
                copy(X2T[:, 0:gr.tiles, :], ps3(TB0, gr), act_Q)

            def stage_R(gr):
                p, n = gr.parity, gr.tiles
                act.wait_ge(*pe_R.done(gr.g))
                act.sem_inc(passed.sem, 1)
                lg = TB1[:, 0:n * E].rearrange("p (t e) -> p t e", e=E)
                copy(XR[:, p, 0:n, D:ROW], lg, act_R)
                copy(LG[:, :, ds(gr.position, n)].rearrange("p e t -> p t e"), lg, act_R)

            def stage_G(slab, c, hy):
                act.wait_ge(*load[slab].done(hy))
                dst = XS[96:KROWS, slab, :].rearrange("p (n q) -> p n q", q=PATCH)
                src = XS[32 * c:32 * c + PATCH, slab, :].rearrange("p (n q) -> p n q", q=PATCH)
                copy(dst[:, :, REST * c:REST * c + REST], src[:, :, PASSES:PATCH], pack[slab])

            for c in range(C):
                stage_G(0, c, 0)
            run(act, {"G": stage_G, "T": stage_T, "X": stage_X, "E": stage_E, "D": stage_D, "S": stage_S, "P": stage_P,
                      "H": stage_H, "L": stage_L, "Q": stage_Q, "R": stage_R})

            act.wait_ge(*dve_f.done(4))
            act.activation(EX, Dm, ACT.Exp, scale=-1.0, accum_out=small[:, 2:3]).then_inc(act_f.sem, 1)

            def one_hot_images(e):
                act.wait_ge(*oh_l.done(e))
                if begun(e - 1):
                    act.wait_ge(*pe_C.done(e - 1))
                act.activation(OHn[:, :, 0, :], OHl, ACT.Copy, scale=iob).then_inc(oh_b.sem, 1)

            def transposed(n, h):
                act.wait_ge(*pe_gt.done(n))
                if begun(n - 2):
                    act.wait_ge(*pe_hid.done(n - 2))
                copy(XGT[:, h, :], bank[1][:, :], act_gt)

            def hidden(n, h, e):
                for f in range(FC):
                    act.wait_ge(*pe_hid.done(n, f + 1))
                    if begun(n - 2):
                        act.wait_ge(*pe_y.done(n - 2))
                        act.sem_inc(passed.sem, 1)
                    act.activation(HT[:, h, f, :], bank[3 + f][:, :], ACT.Gelu,
                                   bias=VT[:, ds(R_B1 + FC * e + f, 1)]).then_inc(act_hid.sem, 1)

            def expert(e, hots, last):
                hidden(2 * e, 0, e)
                transposed(2 * e + 1, 1)
                if hots:
                    one_hot_images(e + 3)
                hidden(2 * e + 1, 1, e)
                if not last:
                    transposed(2 * e + 2, 0)

            one_hot_images(0)
            one_hot_images(1)
            one_hot_images(2)
            transposed(0, 0)
            expert(0, True, False)
            expert(1, True, False)
            with act.Fori(1, E // 2 - 1) as j:
                expert(2 * j, True, False)
                expert(2 * j + 1, True, False)
            expert(E - 2, False, False)
            expert(E - 1, False, True)

        @block.vector
        def _(dve):
            steps = [0]

            def chain(ins):
                steps[0] += 1
                ins.then_inc(dve_pro.sem, 1)
                dve.wait_ge(*dve_pro.done(steps[0] - 1))

            dve.wait_ge(*c_loaded.done(0))
            for c in range(C):
                dve.memset(WP[:, :, 32 * c + PATCH:32 * c + 32], 0.0)
            dve.wait_ge(*w_loaded.done(0))
            wn = WN.rearrange("p (c y q) -> p c q y", c=C, y=PATCH)
            for c in range(C):
                dve.tensor_copy(WP[:, :, 32 * c:32 * c + PATCH], wn[:, c, 0:PASSES, :])
                last = dve.tensor_copy(WP[:, REST * c:REST * c + REST, 96:KROWS], wn[:, c, PASSES:PATCH, :])
            last.then_inc(wp_ready.sem, 1)

            dve.wait_ge(*pro_sig.done(0))
            chain(dve.tensor_scalar(ema_t[:, 0:2, :], ema_t[:, 0:2, :], 1.0, None, ALU.add))
            chain(dve.reciprocal(ema_t[:, 0:2, :], ema_t[:, 0:2, :]))
            chain(dve.tensor_tensor(ema_t[:, 2, :], ema_t[:, 0, :], ema_t[:, 1, :], ALU.mult))
            chain(dve.tensor_scalar(ema_t[:, 2, :], ema_t[:, 2, :], -1.0, 1.0, ALU.mult, ALU.add))
            chain(dve.tensor_copy(qdec[:, :, :], ema_t[:, 2, :].unsqueeze(2).to_broadcast([128, HEADS, 512])))
            chain(dve.memset(qdec[:, :, 0:512:128], 0.0))
            chain(dve.tensor_tensor(ema_t[:, 3, :], ema_t[:, 0, :], ema_in[:, 2, :], ALU.mult))
            chain(dve.tensor_tensor(ema_c[:, :], ema_t[:, 3, :], ema_in[:, 3, :], ALU.mult))
            chain(dve.tensor_scalar(ema_c[:, :], ema_c[:, :], EMA_SCALE, None, ALU.mult))
            chain(dve.tensor_scalar(nbv[:, :], nbv[:, :], -1.0, None, ALU.mult))
            dve.wait_ge(*pro_evac.done(4))
            chain(dve.tensor_scalar(derived[:, 0:1], vcol(R_QKW), QSCALE, None, ALU.mult))
            chain(dve.tensor_scalar(derived[:, 1:2], vcol(R_QKB), QSCALE, None, ALU.mult))
            chain(dve.tensor_tensor(derived[:, 2:3], vcol(R_BMX + 4), vcol(R_BH), ALU.add))
            chain(dve.tensor_scalar(derived[:, 3:4], vcol(R_BMX), 0.5, None, ALU.mult))
            chain(dve.tensor_tensor(tokT[:, 0, :], vcol(R_CLS).to_broadcast([128, 128]),
                                    vcol(R_POS).to_broadcast([128, 128]), ALU.mult))
            dve.memset(stats[:, 0, 0:1], 0.0).then_inc(consts_done.sem, 1)

            def normalise(dst, src, mv, rs, gr):
                for t in range(gr.tiles):
                    last = dve.tensor_scalar(dst(t), src(t), mv[:, gr.parity, t, 0:1], rs[:, gr.parity, t:t + 1],
                                             ALU.subtract, ALU.mult)
                return last

            stats_before = {"T": {0: (dve_M, -1), 1: (dve_T, -1), None: None},
                            "L": {0: (dve_T, 1), 1: (dve_L, -1), None: (dve_T, 0)},
                            "M": {0: (dve_L, 1), 1: (dve_M, -1), None: (dve_L, 0)}}

            def statistics(stage, src, mv, done, gr, k):
                if stats_before[stage][gr.u]:
                    user, ahead = stats_before[stage][gr.u]
                    if begun(gr.g + ahead):
                        dve.wait_ge(*user.done(gr.g + ahead))
                for t in range(gr.tiles):
                    last = dve.bn_stats(stats[:, t, :], src(t))
                last.then_inc(done.sem, 1)
                dve.wait_ge(*done.done(gr.g, k))
                dve.sem_inc(passed.sem, 1)
                for t in range(gr.tiles):
                    last = dve.bn_aggr(mv[:, gr.parity, t, :], stats[:, t, :])
                last.then_inc(done.sem, 1)

            def stage_K(half, hy):
                dve.wait_ge(*pe_tok[half].done(hy))
                dve.wait_ge(*pe_T.done(2 * hy))
                dve.scalar_tensor_tensor(
                    out=tokT[:, :, HALF * half:HALF * half + HALF].rearrange("p w b -> p b w"),
                    in0=TOK[half][:, :].rearrange("p (b w) -> p b w", w=NP), scalar=vcol(R_TOKB),
                    in1=VT[:, ds(R_POS + 1 + hy * NP, NP)].unsqueeze(1).to_broadcast([128, HALF, NP]),
                    op0=ALU.add, op1=ALU.mult).then_inc(dve_K[half].sem, 1)

            def stage_T(gr):
                dve.wait_ge(*act_T.done(gr.g))
                statistics("T", lambda t: H[:, gr.parity, t, :], mvA, dve_T, gr, 1)

            def stage_N(gr):
                dve.wait_ge(*pool_N.done(gr.g))
                if begun(gr.g - 1):
                    dve.wait_ge(*pe_X.done(gr.g - 1))
                if begun(gr.g - 1 if gr.u != 1 else gr.g - 2):
                    dve.wait_ge(*pe_R.done(gr.g - 1 if gr.u != 1 else gr.g - 2))
                normalise(lambda t: X[:, t, :], lambda t: H[:, gr.parity, t, :], mvA, rsA, gr)\
                    .then_inc(dve_N.sem, 1)

            def stage_V(gr):
                if begun(gr.g - 2):
                    dve.wait_ge(*pe_O.done(gr.g - 2))
                for k in range(2):
                    dve.wait_ge(*pe_V.done(gr.g, k + 1))
                    if gr.tiles == 1:
                        c = slice(128 * k, 128 * k + 128)
                        ins = dve.tensor_tensor(Vv[:, gr.parity, 0, c], VB[k][:, 0:128], nbv[:, c], ALU.max)
                    else:
                        ins = dve.tensor_tensor(Vv[:, gr.parity, 2 * k:2 * k + 2, :],
                                                VB[k][:, :].rearrange("p (t v) -> p t v", v=V),
                                                nbv[:, :].unsqueeze(1).to_broadcast([128, 2, V]), ALU.max)
                    ins.then_inc(dve_V.sem, 1)

            def stage_E(gr):
                n, p = gr.cols, gr.parity
                dve.wait_ge(*act_X.done(gr.g))

                def scan(h):
                    dve.tensor_tensor_scan(Y[:, h % 2, 0:n], qdec[:, h, 0:n], XT[:, p, 0:n], 0.0, ALU.mult, ALU.add)\
                        .then_inc(dve_E.sem, 1)

                def add(h, done):
                    dve.wait_ge(*dve_E.done(gr.g, done))
                    dve.scalar_tensor_tensor(out=ET[:, p, 0:n], in0=Y[:, h % 2, 0:n], scalar=ema_c[:, h:h + 1],
                                             in1=ET[:, p, 0:n], op0=ALU.mult, op1=ALU.add).then_inc(dve_E.sem, 1)
                if begun(gr.g - 1):
                    dve.wait_ge(*dve_E.done(gr.g - 1))
                scan(0)
                scan(1)
                dve.wait_ge(*act_E.done(gr.g))
                add(0, 1)
                add(1, 3)
                scan(2)
                dve.wait_ge(*dve_E.done(gr.g, 4))
                scan(3)
                add(2, 5)
                add(3, 7)

            def stage_S(gr):
                p, n = gr.parity, gr.tiles
                dve.wait_ge(*pe_S.done(gr.g))
                if begun(gr.g - 2):
                    dve.wait_ge(*pe_P.done(gr.g - 2))
                dve.tensor_tensor(S[:, p, 0:n, :], DB0[:, 0:gr.cols].rearrange("p (t m) -> p t m", m=128),
                                  relb[:, :].unsqueeze(1).to_broadcast([128, n, 128]), ALU.add)\
                    .then_inc(dve_S.sem, 1)
                dve.wait_ge(*dve_S.done(gr.g, 1))
                if begun(gr.g - 2):
                    dve.wait_ge(*act_S.done(gr.g - 2))
                dve.tensor_reduce(nmax[:, p, 0:n], S[:, p, 0:n, :], AX.X, ALU.max, negate=True)\
                    .then_inc(dve_S.sem, 1)

            def stage_Z(gr):
                p, n = gr.parity, gr.tiles
                dve.wait_ge(*act_S.done(gr.g))
                dve.reciprocal(rsum[:, p, 0:n], ssum[:, p, 0:n]).then_inc(dve_Z.sem, 1)
                dve.wait_ge(*dve_Z.done(gr.g, 1))
                dve.tensor_tensor(S[:, p, 0:n, :], S[:, p, 0:n, :],
                                  rsum[:, p, 0:n].unsqueeze(2).to_broadcast([128, n, 128]), ALU.mult)\
                    .then_inc(dve_Z.sem, 1)

            def stage_O(gr):
                n, p = gr.cols, gr.parity
                dve.wait_ge(*act_D.done(gr.g, 3))
                if begun(gr.g - 1):
                    dve.wait_ge(*pe_H.done(gr.g - 1))
                for c in range(VC):
                    dve.wait_ge(*pe_O.done(gr.g, c + 1))
                    dve.scalar_tensor_tensor(out=G[:, c, 0:n], in0=VB[c][:, 0:n], scalar=vcol(R_BV + c),
                                             in1=GT[:, p, c, 0:n], op0=ALU.add, op1=ALU.mult)\
                        .then_inc(dve_O.sem, 1)

            def stage_H(gr):
                n, p = gr.cols, gr.parity
                dve.wait_ge(*pool_H.done(gr.g))
                dve.wait_ge(*act_D.done(gr.g))
                dve.scalar_tensor_tensor(out=HR[:, 0:n], in0=TH[:, p, 0:n], scalar=1.0, in1=HR[:, 0:n],
                                         op0=ALU.add, op1=ALU.mult).then_inc(dve_H.sem, 1)
                dve.wait_ge(*dve_H.done(gr.g, 1))
                if begun(gr.g - 1):
                    dve.wait_ge(*pe_L.done(gr.g - 1))
                dve.scalar_tensor_tensor(out=OT[:, 0:n], in0=HR[:, 0:n], scalar=0.5, in1=XT[:, p, 0:n],
                                         op0=ALU.mult, op1=ALU.add).then_inc(dve_H.sem, 1)

            def stage_L(gr):
                dve.wait_ge(*act_L.done(gr.g))
                if begun(gr.g - 2):
                    dve.wait_ge(*pool_L.done(gr.g - 2))
                statistics("L", lambda t: O[:, gr.parity, t, :], mvB, dve_L, gr, 1)

            def stage_M(gr):
                p, n = gr.parity, gr.tiles
                o = O[:, p, 0:n, :]
                dve.wait_ge(*pool_L.done(gr.g))
                normalise(lambda t: O[:, p, t, :], lambda t: O[:, p, t, :], mvB, rsB, gr).then_inc(dve_M.sem, 1)
                dve.wait_ge(*dve_M.done(gr.g, 1))
                dve.tensor_tensor(o, o, lnw[:, :].unsqueeze(1).to_broadcast([128, n, D]), ALU.mult)\
                    .then_inc(dve_M.sem, 1)
                dve.wait_ge(*dve_M.done(gr.g, 2))
                dve.wait_ge(*pool_B.done(gr.g))
                dve.tensor_tensor(o, o, H[:, p, 0:n, :], ALU.add).then_inc(dve_M.sem, 1)
                dve.wait_ge(*dve_M.done(gr.g, 3))
                statistics("M", lambda t: O[:, p, t, :], mvC, dve_M, gr, 4)

            def stage_Q(gr):
                p = gr.parity
                dve.wait_ge(*pool_M.done(gr.g))
                if begun(gr.stored - 1):
                    dve.wait_ge(*row_stored[p].done(gr.stored - 1))
                normalise(lambda t: XR[:, p, t, 0:D], lambda t: O[:, p, t, :], mvC, rsC, gr)\
                    .then_inc(dve_Q.sem, 1)

            run(dve, {"K": stage_K, "T": stage_T, "N": stage_N, "V": stage_V, "E": stage_E, "S": stage_S,
                      "Z": stage_Z, "O": stage_O, "H": stage_H, "L": stage_L, "M": stage_M, "Q": stage_Q})

            fsteps = [0]

            def link(ins, wait=True):
                fsteps[0] += 1
                ins.then_inc(dve_f.sem, 1)
                if wait:
                    dve.wait_ge(*dve_f.done(fsteps[0] - 1))

            dve.wait_ge(*ffn_consts.done(0))
            dve.wait_ge(*r_in.done(0))
            link(dve.tensor_reduce(small[:, 0:1], R, AX.X, ALU.max))
            dve.wait_ge(*pe_f.done(0))
            link(dve.tensor_reduce(mrow[0:1, 0:E], bank[0][0:1, 0:128].rearrange("p (e c) -> p e c", e=E),
                                   AX.X, ALU.max))
            link(dve.tensor_copy(junk[0:1, 0:128].rearrange("p (e c) -> p e c", e=E),
                                 mrow[0:1, 0:E].unsqueeze(2).to_broadcast([1, E, 16])))
            dve.wait_ge(*pe_f.done(1))
            link(dve.tensor_copy(small[:, 1:2], bank[0][:, 128:129]))
            link(dve.tensor_scalar(Dm, R, small[:, 1:2], -1.0, ALU.subtract, ALU.mult))
            thr, cand, bit, take = smalli[:, 0:1], smalli[:, 1:2], smalli[:, 2:3], smalli[:, 3:4]
            dve.memset(thr, 0)
            link(dve.memset(bit, 1 << 30))
            with dve.Fori(0, 31) as it:
                dve.tensor_tensor(cand, thr, bit, ALU.bitwise_or).then_inc(step_done.sem, 1)
                dve.wait_ge(*step_done.done(it, 1))
                dve.tensor_scalar(junk, Dm, cand.bitcast(F32), 0.0, ALU.is_lt, ALU.add,
                                  accum_out=small[:, 3:4]).then_inc(cnt_ready.sem, 1)
                dve.tensor_single_scalar(bit, bit, 1, ALU.logical_shift_right).then_inc(step_done.sem, 1)
                dve.wait_ge(*cnt_summed.done(it))
                dve.tensor_scalar(take, bank[0][:, 0:1], float(CAP), None, ALU.is_lt).then_inc(step_done.sem, 1)
                dve.wait_ge(*step_done.done(it, 3))
                dve.sem_inc(passed.sem, 1)
                dve.copy_predicated(thr, take, cand).then_inc(step_done.sem, 1)
                dve.wait_ge(*step_done.done(it, 4))
            tf = thr.bitcast(F32)
            link(dve.tensor_scalar(S1, Dm, tf, 0.0, ALU.is_lt, ALU.add, accum_out=small[:, 4:5]))
            link(dve.tensor_scalar(EQ, Dm, tf, 0.0, ALU.is_equal, ALU.add, accum_out=small[:, 5:6]))
            link(dve.tensor_tensor_scan(CE, EQ, EQ, 0.0, ALU.add, ALU.max))
            dve.wait_ge(*pe_f.done(2))
            link(dve.tensor_scalar(small[:, 6:7], bank[0][:, 1:2], -1.0, float(CAP), ALU.mult, ALU.add))
            link(dve.tensor_copy(small[:, 7:8], bank[0][:, 2:3]))
            link(dve.tensor_scalar(CE, CE, small[:, 7:8], small[:, 6:7], ALU.add, ALU.is_le))
            link(dve.tensor_tensor(EQ, EQ, CE, ALU.mult))
            link(dve.tensor_tensor(S1, S1, EQ, ALU.add))
            link(dve.tensor_tensor_scan(CE, S1, S1, 0.0, ALU.add, ALU.max))
            dve.wait_ge(*act_f.done(0))
            dve.wait_ge(*pe_f.done(3))
            link(dve.tensor_copy(small[:, 8:9], bank[0][:, 3:4]))
            link(dve.scalar_tensor_tensor(out=SLR, in0=CE, scalar=small[:, 8:9], in1=S1, op0=ALU.add,
                                          op1=ALU.mult))
            dve.tensor_scalar(SLR, SLR, -1.0, None, ALU.add).then_inc(slr_ready.sem, 1)
            link(dve.reciprocal(small[:, 9:10], bank[0][:, 4:5]))
            dve.tensor_scalar(msel[:, 0:E], sel0, small[:, 1:2], None, ALU.mult)
            link(dve.tensor_scalar(msel[:, E:2 * E], sel0, small[:, 9:10], None, ALU.mult))
            dve.wait_ge(*pe_f.done(4))
            dve.tensor_copy(MB, bank[0][:, 16:16 + E])
            link(dve.tensor_copy(IS, bank[0][:, 16 + E:16 + 2 * E]))

            dve.wait_ge(*sl_in.done(0))
            link(dve.tensor_copy(SLi, SL.rearrange("p e s -> p (e s)")))
            dve.tensor_single_scalar(HIi, SLi, 5, ALU.arith_shift_right)
            link(dve.tensor_single_scalar(LOi, SLi, 31, ALU.bitwise_and))
            dve.memset(HI[:, E, :], -1.0)
            dve.memset(LO[:, E, :], 0.0)
            dve.tensor_copy(HI[:, 0:E, :].rearrange("p e s -> p (e s)"), HIi)
            dve.tensor_copy(LO[:, 0:E, :].rearrange("p e s -> p (e s)"), LOi).then_inc(hilo.sem, 1)
            dve.wait_ge(*hilo.done(0))

            def one_hots(e):
                if begun(e - 1):
                    dve.wait_ge(*oh_b.done(e - 1))
                if begun(e - 1):
                    dve.wait_ge(*oh_p.done(e - 1))
                i32 = io32.unsqueeze(1).to_broadcast([128, SEQ, 32])
                dve.tensor_tensor(OHl, LO[:, ds(e, 1), :].rearrange("p o s -> p (o s)").unsqueeze(2)
                                  .to_broadcast([128, SEQ, 32]), i32, ALU.is_equal).then_inc(oh_l.sem, 1)
                if begun(e - 1):
                    dve.wait_ge(*pe_C.done(e - 1))
                dve.tensor_tensor(OHh, HI[:, ds(e, 1), :].rearrange("p o s -> p (o s)").unsqueeze(2)
                                  .to_broadcast([128, SEQ, 32]), i32, ALU.is_equal).then_inc(oh_h.sem, 1)
                dve.wait_ge(*oh_l.done(e))
                dve.tensor_tensor(OHn[:, :, 1, :], OHl, ioP[:, 0:SEQ].unsqueeze(2).to_broadcast([128, SEQ, 32]),
                                  ALU.mult).then_inc(oh_p.sem, 1)

            def token_index(e):
                dve.wait_ge(*pe_C.done(e))
                if begun(e - 1):
                    dve.wait_ge(*ix_out.done(e - 1))
                dve.tensor_copy(IXf[0:32, :], bank[0][0:32, 0:64]).then_inc(dve_C.sem, 1)
                dve.wait_ge(*dve_C.done(e, 1))
                dve.scalar_tensor_tensor(out=IX[0:32, :], in0=IXf[0:32, 0:32], scalar=float(SEQ),
                                         in1=IXf[0:32, 32:64], op0=ALU.mult, op1=ALU.add).then_inc(dve_C.sem, 1)

            def differences(e, h, j):
                dve.wait_ge(*gathered[h].done(j))
                dve.tensor_scalar(vdiff[:, h, :], XG[:, h, :, ds(D + e, 1)].rearrange("p k o -> p (k o)"),
                                  MB[:, ds(e, 1)], None, ALU.subtract).then_inc(val_d.sem, 1)

            def probabilities(e, h):
                dve.wait_ge(*val_p.done(e))
                if begun(2 * e - 3):
                    dve.wait_ge(*dve_ow.done(2 * e - 3))
                dve.tensor_scalar(val[:, h, :], vexp[:, h, :], IS[:, ds(e, 1)], None, ALU.mult)\
                    .then_inc(val_r.sem, 1)

            def result(n, h, e):
                dve.wait_ge(*pe_y.done(n))
                if begun(n - 2):
                    dve.wait_ge(*pe_yt.done(n - 2))
                dve.tensor_scalar(YT[:, h, :], bank[7][:, :], VT[:, ds(R_B2 + e, 1)], None, ALU.add)\
                    .then_inc(dve_y.sem, 1)

            def weigh(n, half, h, e):
                dve.wait_ge(*pe_yt.done(n))
                if half == 0:
                    if begun(e - 2):
                        dve.wait_ge(*scattered.done(e - 2))
                    dve.wait_ge(*val_r.done(e))
                dve.tensor_tensor(OW[:, h, 4 * half:4 * half + 4, :],
                                  bank[2][:, :].rearrange("p (k d) -> p k d", d=D),
                                  val[:, h, 4 * half:4 * half + 4].unsqueeze(2).to_broadcast([128, 4, D]),
                                  ALU.mult).then_inc(dve_ow.sem, 1)

            def expert(e, h, j, before, lists, hots, last=False):
                if before:
                    weigh(2 * e - 2, 0, 1 - h, e - 1)
                    result(2 * e - 1, 1, e - 1)
                if lists:
                    token_index(e + 2)
                if hots:
                    one_hots(e + 3)
                if not last:
                    differences(e + 1, 1 - h, j + h)
                if before:
                    weigh(2 * e - 1, 1, 1 - h, e - 1)
                result(2 * e, 0, e)
                if not last:
                    probabilities(e + 1, 1 - h)

            for e in (0, 1):
                one_hots(e)
                token_index(e)
            one_hots(2)
            differences(0, 0, 0)
            probabilities(0, 0)
            expert(0, 0, 0, False, True, True)
            expert(1, 1, 0, True, True, True)
            with dve.Fori(1, E // 2 - 1) as j:
                expert(2 * j, 0, j, True, True, True)
                expert(2 * j + 1, 1, j, True, True, True)
            expert(E - 2, 0, E // 2 - 1, True, False, False)
            expert(E - 1, 1, E // 2 - 1, True, False, False, last=True)
            weigh(2 * E - 2, 0, 1, E - 1)
            result(2 * E - 1, 1, E - 1)
            weigh(2 * E - 1, 1, 1, E - 1)

        @block.tensor
        def _(pe):
            pe.wait_ge(*const_ready.done(0))
            pe.wait_ge(*v_loaded.done(0))
            pe.wait_ge(*m_loaded.done(0))
            pe.transpose(bank[5][:, 0:120], VN[0:120, :], ident[0:120, 0:120])
            for k in range(VC):
                last = pe.transpose(bank[5][:, 128 + 128 * k:256 + 128 * k], WvN[:, k, :], ident[:, :])
            last.then_inc(pe_pro.sem, 1)
            for k in range(4):
                last = pe.transpose(bank[6][:, 128 * k:128 * k + 128], WmN[:, k, :], ident[:, :])
            last.then_inc(pe_pro.sem, 1)
            pe.transpose(bank[7][:, 0:128], WmN[:, 4, :], ident[:, :])
            for k in range(VC):
                pe.transpose(bank[7][:, 128 + 128 * k:256 + 128 * k], WhN[:, 128 * k:128 * k + 128], ident[:, :])
            pe.wait_ge(*c_loaded.done(0))
            last = pe.matmul(bank[7][:, 384:512], flip, relN, start=True, stop=True)
            last.then_inc(pe_pro.sem, 1)
            pe.wait_ge(*wp_ready.done(0))
            for n in range(5):
                for k in range(4):
                    last = pe.transpose(bank[n][0:KROWS, 128 * k:128 * k + 128], WP[:, 4 * n + k, 0:KROWS], ident[:, :])
                last.then_inc(pe_pro.sem, 1)
            pe.wait_ge(*pro_evac.done(1))
            pe.transpose(bank[5][0:KROWS, 384:512], WP[:, 20, 0:KROWS], ident[:, :]).then_inc(pe_pro.sem, 1)
            pe.wait_ge(*pro_evac.done(11))
            pe.wait_ge(*consts_done.done(0))
            pe.wait_ge(*gaps_done.done(0))

            def token_pass(n, i):
                half, t = divmod(n, PASSES)
                if t == 0:
                    pe.wait_ge(*pack[half].done(i))
                    if begun(i - 1):
                        pe.wait_ge(*dve_K[half].done(i - 1))
                ins = pe.matmul(TOK[half][:, :], WT[0:KROWS, t, :],
                                XS[0:KROWS, half, :].rearrange("p (n q) -> p n q", q=PATCH)[:, :, t],
                                start=(t == 0), stop=(t == PASSES - 1))
                if t == PASSES - 1:
                    ins.then_inc(pe_tok[half].sem, 1)

            PASSES_AFTER = {("T", 1): 3, ("X", 1): 1, ("V", 1): 8, ("D", 0): 2, ("S", 0): 2, ("D", 1): 2,
                            ("S", 1): 3, ("H", 1): 5, ("L", 1): 8, ("Q", 1): 5, ("R", 1): 3,
                            ("T", None): 3, ("X", None): 3, ("V", None): 4, ("D", None): 3, ("S", None): 3,
                            ("P", None): 3, ("O", None): 2, ("H", None): 5, ("L", None): 6, ("Q", None): 5,
                            ("R", None): 5}
            place = [0]

            def tokens_after(s, w, i):
                n = PASSES_AFTER.get((s, w.u), 0)
                for _ in range(n):
                    token_pass(place[0], i)
                    place[0] = (place[0] + 1) % (2 * PASSES)

            def tile(t, gr, n):
                return t[:, 128 * n:128 * n + 128]

            def stage_T(gr):
                bank_free(pe, "T", gr)
                if gr.u is not None:
                    for half in range(2):
                        pe.wait_ge(*dve_K[half].done(gr.row))
                for t in range(gr.tiles):
                    last = pe.transpose(tile(TB0, gr, t), tokT[:, (gr.u or 0) * 4 + t, :], ident[:, :])
                last.then_inc(pe_T.sem, 1)

            def stage_X(gr):
                pe.wait_ge(*dve_N.done(gr.g))
                bank_free(pe, "X", gr)
                for t in range(gr.tiles):
                    last = pe.transpose(tile(TB1, gr, t), X[:, t, :], ident[:, :])
                last.then_inc(pe_X.sem, 1)

            def stage_V(gr):
                pe.wait_ge(*act_X.done(gr.g))
                xt = XT[:, gr.parity, :]
                for k in range(2):
                    if gr.u == 0:
                        if begun(gr.g - 1):
                            pe.wait_ge(*dve_O.done(gr.g - 1, k + 1))
                    elif gr.u == 1:
                        if begun(gr.g - 1):
                            pe.wait_ge(*dve_V.done(gr.g - 1, k + 1))
                    if gr.tiles == 1:
                        last = pe.matmul(VB[k][:, 0:128], xt[:, 0:128], WvT[:, 128 * k:128 * k + 128],
                                         start=True, stop=True)
                    else:
                        for t in range(2):
                            a = 128 * (2 * k + t)
                            last = pe.matmul(VB[k][:, V * t:V * t + V], xt[:, a:a + 128], WvT[:, :],
                                             start=True, stop=True)
                    last.then_inc(pe_V.sem, 1)

            def stage_D(gr):
                n = gr.cols
                pe.wait_ge(*relu_E.done(gr.g))
                et = ET[:, gr.parity, 0:n]
                if begun(gr.g - 1):
                    pe.wait_ge(*dve_S.done(gr.g - 1, 1))
                pe.matmul(DB0[:, 0:n], WmT[:, 1, :], et, start=True, stop=True).then_inc(pe_D.sem, 1)
                if gr.u == 0:
                    if begun(gr.g - 1):
                        pe.wait_ge(*act_H.done(gr.g - 1))
                elif gr.u == 1:
                    if begun(gr.g - 1):
                        pe.wait_ge(*act_D.done(gr.g - 1, 4))
                pe.matmul(DB1[:, 0:n], WmT[:, 2, :], et, start=True, stop=True).then_inc(pe_D.sem, 1)
                pe.wait_ge(*act_D.done(gr.g, 1))
                pe.matmul(DB0[:, 0:n], WmT[:, 3, :], et, start=True, stop=True).then_inc(pe_D.sem, 1)
                pe.wait_ge(*act_D.done(gr.g, 2))
                pe.matmul(DB1[:, 0:n], WmT[:, 0, :], et, start=True, stop=True).then_inc(pe_D.sem, 1)

            def stage_S(gr):
                pe.wait_ge(*pool_D.done(gr.g))
                pe.wait_ge(*act_D.done(gr.g, 3))
                for t in range(gr.tiles):
                    last = pe.matmul(tile(DB0, gr, t), tile(QT, gr, t), tile(QKT, gr, t), start=True, stop=True)
                last.then_inc(pe_S.sem, 1)

            def stage_P(gr):
                pe.wait_ge(*dve_Z.done(gr.g))
                bank_free(pe, "P", gr)
                for t in range(gr.tiles):
                    last = pe.transpose(tile(TB0, gr, t), S[:, gr.parity, t, :], ident[:, :])
                last.then_inc(pe_P.sem, 1)

            def stage_O(gr):
                pe.wait_ge(*act_P.done(gr.g))
                for c in range(VC):
                    if gr.u == 0:
                        pe.wait_ge(*dve_V.done(gr.g + 1, c + 1))
                    elif gr.u == 1:
                        if begun(gr.g - 1):
                            pe.wait_ge(*dve_O.done(gr.g - 1, c + 1))
                    else:
                        pe.wait_ge(*dve_V.done(gr.g))
                    for t in range(gr.tiles):
                        last = pe.matmul(tile(VB[c], gr, t), Vv[:, gr.parity, t, 128 * c:128 * c + 128],
                                         tile(PT, gr, t), start=True, stop=True)
                    last.then_inc(pe_O.sem, 1)

            def stage_H(gr):
                n = gr.cols
                pe.wait_ge(*act_D.done(gr.g + 1 if gr.u == 0 else gr.g, 4))
                if gr.u == 1:
                    if begun(gr.g - 1):
                        pe.wait_ge(*act_H.done(gr.g - 1))
                pe.matmul(DB1[:, 0:n], WmT[:, 4, :], ET[:, gr.parity, 0:n], start=True, stop=False)
                for c in range(VC):
                    pe.wait_ge(*dve_O.done(gr.g, c + 1))
                    last = pe.matmul(DB1[:, 0:n], WhT[:, c, :], G[:, c, 0:n], start=False, stop=(c == VC - 1))
                last.then_inc(pe_H.sem, 1)

            def stage_L(gr):
                pe.wait_ge(*dve_H.done(gr.g))
                bank_free(pe, "L", gr)
                for t in range(gr.tiles):
                    last = pe.transpose(tile(TB1, gr, t), tile(OT, gr, t), ident[:, :])
                last.then_inc(pe_L.sem, 1)

            def stage_Q(gr):
                pe.wait_ge(*dve_Q.done(gr.g))
                bank_free(pe, "Q", gr)
                for t in range(gr.tiles):
                    last = pe.transpose(tile(TB0, gr, t), XR[:, gr.parity, t, 0:D], ident[:, :])
                last.then_inc(pe_Q.sem, 1)

            def stage_R(gr):
                pe.wait_ge(*act_Q.done(gr.g))
                bank_free(pe, "R", gr)
                for t in range(gr.tiles):
                    last = pe.matmul(TB1[:, E * t:E * t + E], X2T[:, t, :], Wr[:, :], start=True, stop=True)
                last.then_inc(pe_R.sem, 1)

            run(pe, {"T": stage_T, "X": stage_X, "V": stage_V, "D": stage_D, "S": stage_S, "P": stage_P,
                     "O": stage_O, "H": stage_H, "L": stage_L, "Q": stage_Q, "R": stage_R}, tokens_after)

            pe.wait_ge(*dve_f.done(0))
            pe.transpose(bank[0][0:1, 0:128], small[:, 0:1], ident[:, :]).then_inc(pe_f.sem, 1)
            pe.wait_ge(*dve_f.done(2))
            pe.matmul(bank[0][:, 128:129], junk[0:1, 0:128], ones[0:1, 0:1], start=True, stop=True)\
                .then_inc(pe_f.sem, 1)
            with pe.Fori(0, 31) as it:
                pe.wait_ge(*cnt_ready.done(it))
                pe.matmul(bank[0][:, 0:1], blk, small[:, 3:4], start=True, stop=True).then_inc(cnt_summed.sem, 1)
            pe.wait_ge(*dve_f.done(7))
            pe.matmul(bank[0][:, 1:2], blk, small[:, 4:5], start=True, stop=True)
            pe.matmul(bank[0][:, 2:3], low, small[:, 5:6], start=True, stop=True).then_inc(pe_f.sem, 1)
            pe.wait_ge(*dve_f.done(14))
            pe.wait_ge(*act_f.done(0))
            pe.matmul(bank[0][:, 3:4], low, CE[:, 519:520], start=True, stop=True)
            pe.matmul(bank[0][:, 4:5], blk, small[:, 2:3], start=True, stop=True).then_inc(pe_f.sem, 1)
            pe.wait_ge(*dve_f.done(18))
            pe.matmul(bank[0][:, 16:32], ones, msel, start=True, stop=True).then_inc(pe_f.sem, 1)

            def compact(e):
                pe.wait_ge(*oh_h.done(e))
                pe.wait_ge(*oh_b.done(e))
                pe.wait_ge(*oh_p.done(e))
                if begun(e - 1):
                    pe.wait_ge(*dve_C.done(e - 1, 1))
                for s in range(SEQ):
                    last = pe.matmul(bank[0][0:32, 0:64], OHh[:, s, :], OHn[:, s, :, :].rearrange("p t h -> p (t h)"),
                                     start=(s == 0), stop=(s == SEQ - 1))
                last.then_inc(pe_C.sem, 1)

            def rows_in(n, half, h, j):
                pe.wait_ge(*gathered[h].done(j))
                if begun(n - 1):
                    pe.wait_ge(*act_gt.done(n - 1))
                for k in range(4):
                    last = pe.transpose(bank[1][:, 128 * k:128 * k + 128], XG[:, h, 4 * half + k, 0:D], ident[:, :])
                last.then_inc(pe_gt.sem, 1)

            def hidden(n, half, h, j):
                pe.wait_ge(*w_in[h].done(j))
                pe.wait_ge(*act_gt.done(n))
                for f in range(FC):
                    if begun(n - 1):
                        pe.wait_ge(*act_hid.done(n - 1, f + 1))
                    pe.matmul(bank[3 + f][:, :], W1s[:, h, 128 * f:128 * f + 128], XGT[:, half, :],
                              start=True, stop=True).then_inc(pe_hid.sem, 1)

            def result(n, half, h):
                if begun(n - 1):
                    pe.wait_ge(*dve_y.done(n - 1))
                for f in range(FC):
                    pe.wait_ge(*act_hid.done(n, f + 1))
                    last = pe.matmul(bank[7][:, :], W2s[:, h, f, :], HT[:, half, f, :], start=(f == 0),
                                     stop=(f == FC - 1))
                last.then_inc(pe_y.sem, 1)

            def rows_out(n, half):
                pe.wait_ge(*dve_y.done(n))
                if begun(n - 1):
                    pe.wait_ge(*dve_ow.done(n - 1))
                for k in range(4):
                    last = pe.transpose(bank[2][:, 128 * k:128 * k + 128], YT[:, half, 128 * k:128 * k + 128],
                                        ident[:, :])
                last.then_inc(pe_yt.sem, 1)

            def expert(e, h, j, before, lists, last):
                if lists:
                    compact(e + 2)
                hidden(2 * e, 0, h, j)
                rows_in(2 * e + 1, 1, h, j)
                if before:
                    rows_out(2 * e - 2, 0)
                    result(2 * e - 1, 1, 1 - h)
                hidden(2 * e + 1, 1, h, j)
                if not last:
                    rows_in(2 * e + 2, 0, 1 - h, j + h)
                if before:
                    rows_out(2 * e - 1, 1)
                result(2 * e, 0, h)

            compact(0)
            compact(1)
            rows_in(0, 0, 0, 0)
            expert(0, 0, 0, False, True, False)
            expert(1, 1, 0, True, True, False)
            with pe.Fori(1, E // 2 - 1) as j:
                expert(2 * j, 0, j, True, True, False)
                expert(2 * j + 1, 1, j, True, True, False)
            expert(E - 2, 0, E // 2 - 1, True, False, False)
            expert(E - 1, 1, E // 2 - 1, True, False, True)
            rows_out(2 * E - 2, 0)
            result(2 * E - 1, 1, 1)
            rows_out(2 * E - 1, 1)


_INS = ['x', 'L0_tok_W', 'L0_tok_b', 'L0_tok_class_token', 'L0_tok_pos_embed', 'L0_attn_proj_v_w',
        'L0_attn_proj_v_b', 'L0_attn_proj_mx_w', 'L0_attn_proj_mx_b', 'L0_attn_proj_h_w', 'L0_attn_proj_h_b',
        'L0_attn_qk_weight', 'L0_attn_qk_bias', 'L0_attn_damping_factor', 'L0_attn_decay_factor',
        'L0_attn_ema_expansion', 'L0_attn_ema_kernel_proj', 'L0_attn_ema_residual_w',
        'L0_attn_rel_pos_bias_w', 'L0_attn_ln_w', 'L0_attn_ln_b', 'L0_ffn_Wr', 'L0_ffn_W1', 'L0_ffn_b1',
        'L0_ffn_W2', 'L0_ffn_b2']


def kernel(**inputs):
    import numpy as np
    import concourse.bacc as bacc
    from concourse.bass_utils import run_bass_kernel_spmd

    nc = bacc.Bacc("TRN2", target_bir_lowering=False, num_devices=1)
    arrays, args = {}, []
    for name in _INS:
        a = np.ascontiguousarray(inputs[name])
        arrays[f"in_{name}"] = a
        args.append(nc.dram_tensor(f"in_{name}", a.shape, mybir.dt.from_np(a.dtype), kind="ExternalInput").ap())
    shape = (inputs['x'].shape[0],) + tuple(inputs['L0_tok_pos_embed'].shape)
    out = nc.dram_tensor("out_0", shape, mybir.dt.float32, kind="ExternalOutput").ap()
    vit_tower(nc, *args, out)
    r = run_bass_kernel_spmd(nc, [arrays], core_ids=[0])
    return r.results[0]["out_0"]
```
